# Optimizing a Trainium2 kernel written in Bass

```python
import numpy as np
import jax
import jax.numpy as jnp

def _softmax(x, axis=-1):
    return jax.nn.softmax(x, axis=axis)

def _gelu(x):
    return jax.nn.gelu(x, approximate=True)

def _silu(x):
    return jax.nn.silu(x)

def _sigmoid(x):
    return jax.nn.sigmoid(x)

def _layernorm(x, axis=-1, eps=1e-05):
    m = jnp.mean(x, axis=axis, keepdims=True)
    v = jnp.var(x, axis=axis, keepdims=True)
    return (x - m) / jnp.sqrt(v + eps)

def _scatter_add(tgt, idx, src, axis=0):
    return tgt.at[idx].add(src)

def _segment_sum(src, seg, n):
    return jax.ops.segment_sum(src, seg, n)
kernel_name = 'mk_xattn_ffn_d1_seqx_r4_cf22a3'

def setup_inputs(seed: int=0):
    np.random.seed(seed)
    _w = jnp.asarray

    def _rec_inputs():
        import jax
        import jax.numpy as jnp
        _rk = jax.random.key(seed)
        x = -0.0002928 + 1 * jax.random.normal(jax.random.fold_in(_rk, 1), (16, 256, 256), jnp.float32)
        _lenS = 256 - jax.random.randint(jax.random.fold_in(_rk, 7), (16,), 0, max(1, 256 // 4) + 1, jnp.int32)
        _lenS2 = 256 - jax.random.randint(jax.random.fold_in(_rk, 8), (16,), 0, max(1, 256 // 4) + 1, jnp.int32)
        _ctx_1024P = jax.random.normal(jax.random.fold_in(_rk, 11), (16, 16, 256), jnp.float32)
        _ctx_1024c = jax.random.dirichlet(jax.random.fold_in(_rk, 511), 0.3 * jnp.ones((16,), jnp.float32), (16, 256))
        _ctx_1024t = jnp.einsum('bsk,bkd->bsd', _ctx_1024c, _ctx_1024P)
        _ctx_1024t = _ctx_1024t * jax.lax.rsqrt(jnp.mean(jnp.square(_ctx_1024t)) + 1e-12) * 0.953939
        ctx_1024 = -1.39393e-06 + 0.999914 * (_ctx_1024t + 0.3 * jax.random.normal(jax.random.fold_in(_rk, 611), (16, 256, 256), jnp.float32))
        return (x, ctx_1024)
    x, ctx_1024 = _rec_inputs()

    def _L0_xattn_setup():
        import jax, jax.numpy as jnp
        import numpy as np
        B, T, N_EMBD, N_HEAD = (2, 512, 256, 16)
        HEAD = N_EMBD // N_HEAD
        WINDOW = 64
        key = jax.random.key(seed)
        kq, kk, kv, kw = jax.random.split(key, 4)
        q = jax.random.normal(kq, (B, T, N_EMBD), dtype=jnp.float32)
        k = jax.random.normal(kk, (B, T, N_EMBD), dtype=jnp.float32)
        v = jax.random.normal(kv, (B, T, N_EMBD), dtype=jnp.float32)
        W_proj = jax.random.normal(kw, (N_EMBD, N_EMBD), dtype=jnp.float32) * (1.0 / np.sqrt(N_EMBD))
        b_proj = jnp.zeros((N_EMBD,), dtype=jnp.float32)
        return {'q': q, 'k': k, 'v': v, 'W_proj': W_proj, 'b_proj': b_proj}
    _L0_xattn_all = _L0_xattn_setup()
    _L0_xattn_in = {k: v for k, v in _L0_xattn_all.items() if k in ('W_proj', 'b_proj')}
    del _L0_xattn_all

    def _L0_ffn_setup():
        import jax, jax.numpy as jnp
        import numpy as np
        DIM = 256
        HIDDEN = 768
        SCALE = 1.0 / 127.0

        def _dequant(w_int, dtype):
            return w_int.astype(dtype) * jnp.asarray(SCALE, dtype)
        key = jax.random.key(seed)
        k_x, k_g, k_u, k_d = jax.random.split(key, 4)
        x = jax.random.normal(k_x, (4, 512, DIM), dtype=jnp.float32)
        w_gate = jax.random.randint(k_g, (HIDDEN, DIM), -127, 128, dtype=jnp.int32)
        w_up = jax.random.randint(k_u, (HIDDEN, DIM), -127, 128, dtype=jnp.int32)
        w_down = jax.random.randint(k_d, (DIM, HIDDEN), -127, 128, dtype=jnp.int32)
        return {'x': x, 'w_gate': w_gate, 'w_up': w_up, 'w_down': w_down}
    _L0_ffn_all = _L0_ffn_setup()
    _L0_ffn_in = {k: v for k, v in _L0_ffn_all.items() if k in ('w_gate', 'w_up', 'w_down')}
    del _L0_ffn_all
    return {'x': x, 'ctx_1024': ctx_1024, 'L0_xattn_W_proj': _L0_xattn_in['W_proj'], 'L0_xattn_b_proj': _L0_xattn_in['b_proj'], 'L0_ffn_w_gate': _L0_ffn_in['w_gate'], 'L0_ffn_w_up': _L0_ffn_in['w_up'], 'L0_ffn_w_down': _L0_ffn_in['w_down']}

def reference(x, ctx_1024, L0_xattn_W_proj, L0_xattn_b_proj, L0_ffn_w_gate, L0_ffn_w_up, L0_ffn_w_down):
    import jax
    import jax.numpy as jnp

    def _L0_xattn_ref(q, k, v, W_proj, b_proj):
        import jax, jax.numpy as jnp
        import numpy as np
        B, T, N_EMBD, N_HEAD = (2, 512, 256, 16)
        HEAD = N_EMBD // N_HEAD
        WINDOW = 64
        Bsz, Tlen, _ = q.shape
        qh = q.reshape(Bsz, Tlen, N_HEAD, HEAD).transpose(0, 2, 1, 3)
        kh = k.reshape(Bsz, Tlen, N_HEAD, HEAD).transpose(0, 2, 1, 3)
        vh = v.reshape(Bsz, Tlen, N_HEAD, HEAD).transpose(0, 2, 1, 3)
        scale = 1.0 / np.sqrt(HEAD)
        scores = jnp.einsum('bhqd,bhkd->bhqk', qh, kh) * scale
        idx = jnp.arange(Tlen)
        dist = jnp.abs(idx[None, :] - idx[:, None])
        scores = jnp.where(dist[None, None] > WINDOW, -jnp.inf, scores)
        attn = jax.nn.softmax(scores, axis=-1)
        y = jnp.einsum('bhqk,bhkd->bhqd', attn, vh)
        y = y.transpose(0, 2, 1, 3).reshape(Bsz, Tlen, N_EMBD)
        return y @ W_proj.T + b_proj

    def _L0_ffn_ref(x, w_gate, w_up, w_down):
        import jax, jax.numpy as jnp
        import numpy as np
        DIM = 256
        HIDDEN = 768
        SCALE = 1.0 / 127.0

        def _dequant(w_int, dtype):
            return w_int.astype(dtype) * jnp.asarray(SCALE, dtype)
        wg = _dequant(w_gate, x.dtype)
        wu = _dequant(w_up, x.dtype)
        wd = _dequant(w_down, x.dtype)
        gate = jnp.einsum('bsd,hd->bsh', x, wg)
        up = jnp.einsum('bsd,hd->bsh', x, wu)
        h = jax.nn.silu(gate) * up
        return jnp.einsum('bsh,dh->bsd', h, wd)
    x = x + _L0_xattn_ref(_layernorm(x, axis=-1), ctx_1024, ctx_1024, L0_xattn_W_proj, L0_xattn_b_proj)
    x = x + _L0_ffn_ref(_layernorm(x, axis=-1), L0_ffn_w_gate, L0_ffn_w_up, L0_ffn_w_down)
    return x

_drawn_inputs = setup_inputs


def setup_inputs(seed=0):
    import zlib

    import numpy as np

    out = dict(_drawn_inputs(seed))
    spreads = {'L0_xattn_b_proj': (0.0, 0.1)}
    factors = {}
    for name, (base, spread) in spreads.items():
        noise = np.random.default_rng([zlib.crc32(name.encode()), seed]).standard_normal(out[name].shape)
        drawn = base * np.exp(spread * noise) if base else spread * noise
        out[name] = jnp.asarray(drawn.astype(out[name].dtype))
    for name, factor in factors.items():
        out[name] = (out[name] * factor).astype(out[name].dtype)
    return out
```

```python
from contextlib import ExitStack

import concourse.bass as bass
from concourse import mybir

F32 = mybir.dt.float32
F32R = mybir.dt.float32r
F16 = mybir.dt.float16
BF16 = mybir.dt.bfloat16
I32 = mybir.dt.int32
ALU = mybir.AluOpType
ACT = mybir.ActivationFunctionType
AX_X = mybir.AxisListType.X

P = 128


def block_kernel(nc, x_in, ctx_in, w_proj, b_proj, w_gate, w_up, w_down, out):
    B, T, D = x_in.shape
    HID = w_gate.shape[0]
    HEADS, WINDOW = 16, 64
    DH = D // HEADS
    QT = T // P
    DT = D // P
    HT = HID // P
    NT = B * QT
    BAND = P + WINDOW
    EPS = 1e-5
    WSCALE = 1.0 / 127.0
    assert T == 2 * P and D == 2 * P and WINDOW == P // 2 and DH == 16

    ROWS = 6 * DH
    SHIFT = ROWS
    ALLROWS = ROWS + 2
    GROUP = 4
    NG = HEADS // GROUP
    VW = 32
    HALF = HEADS // 2
    LOADS = 6
    ST_LAG = 12
    AV_LAG = ST_LAG + 8
    NS, NST = 2, 3

    def tile(m, i):
        return m[:, i, :] if isinstance(i, int) else m[:, bass.ds(i, 1), :].rearrange("p a d -> p (a d)")

    def one(m, i, k):
        return m[:, i, k:k + 1] if isinstance(i, int) else m[:, bass.ds(i, 1), k:k + 1].rearrange("p a d -> p (a d)")

    def col(m, i):
        return m[:, i:i + 1] if isinstance(i, int) else m[:, bass.ds(i, 1)]

    def wait_apart(engine, semaphore, value, counter):
        engine.wait_ge(semaphore, value)
        engine.sem_inc(counter, 1)

    ctx = ExitStack()
    with ctx:
        def sb(name, shape, dt, stack=ctx):
            return stack.enter_context(nc.sbuf_tensor(name, shape, dt))

        def sem(name, stack=ctx):
            return stack.enter_context(nc.semaphore(name))

        psum = ctx.enter_context(nc.psum_tensor("psum", [P, 8, 512], F32))

        X = sb("X", [P, NT, D], F32)
        ident = sb("ident", [P, P], F32)
        wgT = sb("wgT", [P, DT, HID], F16)
        wuT = sb("wuT", [P, DT, HID], F16)
        wdT = sb("wdT", [P, HT, D], F32R)
        mv2 = sb("mv2", [P, NT, 2], F32)
        rstd2 = sb("rstd2", [P, NT], F32)
        eps = sb("eps", [P, 1], F32)

        with ExitStack() as a:
            ctxs = sb("ctxs", [P, 2, QT, D], F32, a)
            Q6 = sb("Q6", [P, 2, HEADS, T], BF16, a)
            K6 = sb("K6", [P, 2, HEADS, T], BF16, a)
            probs = sb("probs", [P, HEADS, 2 * BAND], F32, a)
            vals = sb("vals", [P, 2, QT, HEADS, VW], F32, a)
            identb = sb("identb", [P, P], BF16, a)
            maskb = sb("maskb", [P, 2 * BAND], BF16, a)
            wraw = sb("wraw", [P, 3, HT * D], I32, a)
            wpraw = sb("wpraw", [P, DT, D], F32, a)
            wpT = sb("wpT", [P, DT, D], F32, a)
            bias = sb("bias", [P, D], F32, a)
            st1 = sb("st1", [P, NT, 6], F32, a)
            mv1 = sb("mv1", [P, NT, 2], F32, a)
            std1 = sb("std1", [P, NT], F32, a)
            rstd1 = sb("rstd1", [P, NT], F32, a)
            st2 = sb("st2", [P, 6], F32, a)
            mvq = sb("mvq", [P, 2], F32, a)
            xn = sb("xn", [P, QT, D], F32, a)
            cn = sb("cn", [P, QT, D], F32, a)
            parts = sb("parts", [P, 2, 3, DT, T], BF16, a)
            rest = sb("rest", [P, 2, DT, T], F32, a)
            maxs = sb("maxs", [P, 2, QT, HEADS], F32, a)
            neg = sb("neg", [P, NG, QT, 2, GROUP], BF16, a)
            negT = sb("negT", [2 * GROUP, NG, T], BF16, a)
            heads = sb("heads", [P, 2, NG, T], F32, a)
            inv = sb("inv", [P, HEADS], F32, a)
            y = sb("y", [P, HEADS, DH], F32, a)
            yT = sb("yT", [P, DT, P], F32, a)
            scr = nc.dram_tensor("parts_scratch", [2, 2, 3, D, T], BF16, kind="Internal").ap()

            XL = 4
            s_x = [sem(f"x_loaded{i}", a) for i in range(B // XL)]
            s_w = sem("weights_loaded", a)
            s_wpool, s_wsp, s_wdve = (sem(f"waits_of_{e}", a) for e in ("pool", "sp", "dve"))
            s_ctx = [sem(f"ctx_loaded{i}", a) for i in range(2)]
            s_const = sem("constants_ready", a)
            s_ones = sem("ones_rows_ready", a)
            s_wf = sem("weights_float", a)
            s_wt = sem("weights_transposed", a)
            s_wc = sem("weights_copied", a)
            s_st = sem("stats_done", a)
            s_std = sem("std_done", a)
            s_rstd = sem("rstd_done", a)
            s_norm = sem("normed", a)
            s_cn = sem("context_ordered", a)
            s_inT = sem("inputs_transposed", a)
            s_p1 = sem("part1_done", a)
            s_r1 = sem("rest1_done", a)
            s_p2 = sem("part2_done", a)
            s_p3 = sem("part3_done", a)
            s_sto = sem("parts_stored", a)
            s_op = [sem(f"operands_loaded{i}", a) for i in range(2)]
            s_S = sem("scores_ready", a)
            s_max = sem("max_done", a)
            s_n1 = sem("neg_high_done", a)
            s_n2 = sem("neg_low_done", a)
            s_nT = sem("neg_transposed", a)
            s_nr = sem("neg_rows_ready", a)
            s_sh = [sem(f"shift_landed{i}", a) for i in range(2)]
            s_ST = sem("scoresT_ready", a)
            s_P = sem("probs_ready", a)
            s_mk = sem("probs_masked", a)
            s_v = sem("vals_ready", a)
            s_av = sem("heads_summed", a)
            s_ho = sem("heads_copied", a)
            s_hT = sem("heads_transposed", a)
            s_inv = sem("sums_inverted", a)
            s_y = sem("y_ready", a)
            s_yT = sem("y_transposed", a)
            s_yc = sem("yT_copied", a)
            s_pr = sem("projected", a)
            s_x1 = sem("x1_ready", a)
            s_bx = sem("bias_added", a)
            s_st2 = sem("stats2_done", a)
            s_mv2 = sem("mv2_done", a)

            bank_in, bank_y, bank_av = psum[:, 5, :], psum[:, 6, :], psum[:, 7, :]

            bank_neg = bank_in.bitcast(BF16)[0:2 * GROUP, 0:T]

            def bank_s(h):
                return psum[:, h % NS, :]

            def bank_st(n):
                return psum[:, NS + n % NST, :]

            def x_rows(b0, nb):
                return x_in[b0:b0 + nb].rearrange("b (q p) d -> p (b q) d", p=P)

            def steps(fixed, looped):
                first, last = 4, 4 + 2 * ((B - 1 - 4) // 2)
                for c in range(-1, first):
                    fixed(c)
                looped(first, last)
                for c in range(last, B + 2):
                    fixed(c)

            def both(body, fori):
                def looped(first, last):
                    with fori(first, last - 1, 2) as c:
                        body(c, 0, None)
                        body(c + 1, 1, None)
                steps(lambda c: body(c, c % 2, c), looped)

            def live(fixed, lag):
                return fixed is None or 0 <= fixed - lag < B

            with nc.Block() as block:

                @block.gpsimd
                def _(pool):
                    nc.gpsimd.memset(ident[:], 0.0).then_inc(s_const, 1)
                    nc.gpsimd.memset(identb[:], 0.0).then_inc(s_const, 1)
                    nc.gpsimd.memset(maskb[:], 0.0).then_inc(s_const, 1)
                    nc.gpsimd.memset(vals[:], 1.0).then_inc(s_const, 1)
                    nc.gpsimd.memset(eps[:], EPS).then_inc(s_const, 1)
                    pool.wait_ge(s_const, 5)
                    for m in (ident, identb):
                        nc.gpsimd.affine_select(out=m[:], in_=m[:], compare_op=ALU.not_equal, fill=1.0,
                                                base=0, pattern=[[-1, P]], channel_multiplier=1).then_inc(s_const, 1)
                    for i, (t, base, step, cm) in enumerate([(0, WINDOW, -1, 1), (0, WINDOW, 1, -1),
                                                             (1, 0, 1, -1), (1, P, -1, 1)]):
                        m = maskb[:, t * BAND:(t + 1) * BAND]
                        pool.wait_ge(s_const, 7 + i)
                        nc.gpsimd.affine_select(out=m, in_=m, compare_op=ALU.is_ge, fill=-1e30, base=base,
                                                pattern=[[step, BAND]], channel_multiplier=cm).then_inc(s_const, 1)

                    def body(c, par, fixed):
                        for h in range(HEADS):
                            g = (h - ST_LAG - GROUP) // GROUP % NG
                            lag = -((h - ST_LAG - GROUP) // HEADS)
                            if h % GROUP == 0 and live(fixed, lag):
                                wait_apart(pool, s_P, (c - lag) * HEADS + GROUP * (g + 1), s_wpool)
                                for lo, n, base, step, cm in ((0, WINDOW, WINDOW, 1, -1),
                                                              (WINDOW, P, 0, -1, 1),
                                                              (BAND, P, 0, 1, -1),
                                                              (BAND + P, WINDOW, 0, -1, 1)):
                                    p = probs[:, GROUP * g:GROUP * (g + 1), lo:lo + n]
                                    nc.gpsimd.affine_select(
                                        out=p, in_=p, compare_op=ALU.is_ge, fill=0.0, base=base,
                                        pattern=[[0, GROUP], [step, n]], channel_multiplier=cm).then_inc(s_mk, 1)
                            if h in (6, 10) and live(fixed, -1):
                                t = (6, 10).index(h)
                                pool.wait_ge(s_p2, 2 * (c + 1) + t + 1)
                                nc.gpsimd.tensor_tensor(parts[:, t, 2], rest[:, t], parts[:, t, 1],
                                                        ALU.subtract).then_inc(s_p3, 1)

                    both(body, pool.Fori)

                @block.sync
                def _(sp):
                    for b0 in range(0, B, XL):
                        sp.dma_start(X[:, b0 * QT:(b0 + XL) * QT, :], x_rows(b0, XL)).then_inc(s_x[b0 // XL], 16)

                    def shift(c, par, fixed, g, lag):
                        if live(fixed, lag):
                            p = (par + lag) % 2
                            sp.wait_ge(s_nr, (c - lag) * NG + g + 1)
                            sp.dma_start(Q6[SHIFT:ALLROWS, p, GROUP * g:GROUP * (g + 1), :],
                                         negT[:, g, :]).then_inc(s_sh[g % 2], 16)

                    def store(c, par, fixed, t):
                        if live(fixed, -1):
                            sp.wait_ge(s_p3, 2 * (c + 1) + t + 1)
                            sp.dma_start(scr[t, 1 - par].rearrange("s (a p) t -> p (s a) t", p=P),
                                         parts[:, t].rearrange("p s a t -> p (s a) t")).then_inc(s_sto, 16)

                    def load(c, par, fixed, half, t):
                        hs = slice(half * HALF, (half + 1) * HALF)
                        if not live(fixed, -1):
                            return
                        o = 1 - par
                        if t == 0 and (fixed is None or fixed >= 1):
                            wait_apart(sp, s_ST, (c - 1) * HEADS + (half + 1) * HALF, s_wsp)
                        if half == 0:
                            sp.wait_ge(s_sto, 16 * (2 * (c + 1) + t + 1))

                        def rows(s, n):
                            if t == 0:
                                v = scr[t, o, s].rearrange("(d h) t -> d h t", h=HEADS)[:, hs, :]
                                v = v.rearrange("d h t -> d (h t)")
                                return bass.AP(tensor=v.tensor, offset=v.offset, ap=[[0, n]] + [list(z) for z in v.ap])
                            v = scr[t, o, s:s + n].rearrange("s (d h) t -> (s d) h t", h=HEADS)
                            return v[:, hs, :].rearrange("p h t -> p (h t)")
                        for slot, s, n in (((0, 0, 3), (3, 1, 2), (5, 2, 1)), ((0, 0, 3), (3, 0, 2), (5, 0, 1)))[t]:
                            sp.dma_start((Q6, K6)[t][slot * DH:(slot + n) * DH, o, hs, :].rearrange("p h t -> p (h t)"),
                                         rows(s, n)).then_inc(s_op[half], 16)

                    def body(c, par, fixed):
                        shift(c, par, fixed, 3, 1)
                        store(c, par, fixed, 0)
                        shift(c, par, fixed, 0, 0)
                        load(c, par, fixed, 0, 0)
                        store(c, par, fixed, 1)
                        shift(c, par, fixed, 1, 0)
                        load(c, par, fixed, 0, 1)
                        shift(c, par, fixed, 2, 0)
                        load(c, par, fixed, 1, 0)
                        load(c, par, fixed, 1, 1)

                    both(body, sp.Fori)

                @block.scalar
                def _(act):
                    act.dma_start(ctxs[:, 0], ctx_in[0].rearrange("(q p) d -> p q d", p=P)).then_inc(s_ctx[0], 16)
                    act.dma_start(wpraw[:], w_proj.rearrange("(a p) d -> p a d", p=P)).then_inc(s_w, 16)
                    for i, w in enumerate((w_gate, w_up)):
                        act.dma_start(wraw[:, i].rearrange("p (a d) -> p a d", d=D),
                                      w.rearrange("(a p) d -> p a d", p=P)).then_inc(s_w, 16)
                    act.dma_start(wraw[:, 2].rearrange("p (a d) -> p a d", d=HID),
                                  w_down.rearrange("(a p) d -> p a d", p=P)).then_inc(s_w, 16)
                    act.dma_start(bias[:], b_proj.partition_broadcast(P)).then_inc(s_w, 16)
                    act.dma_start(ctxs[:, 1], ctx_in[1].rearrange("(q p) d -> p q d", p=P)).then_inc(s_ctx[1], 16)
                    act.wait_ge(s_w, 80)
                    for i in range(3):
                        nc.scalar.activation(wraw[:, i].bitcast(F32), wraw[:, i], ACT.Copy).then_inc(s_wf, 1)
                    act.wait_ge(s_st, 2 * NT)
                    act.wait_ge(s_const, 5)
                    nc.scalar.activation(std1[:], mv1[:, :, 1], ACT.Sqrt, bias=eps[:]).then_inc(s_std, 1)

                    def body(c, par, fixed):
                        for h in range(HEADS):
                            k = h - AV_LAG - 1
                            lag, g = -(k // HEADS), k % HEADS // GROUP
                            if k % GROUP == GROUP - 1 and live(fixed, lag):
                                act.wait_ge(s_av, (c - lag) * HEADS + GROUP * (g + 1))
                                if fixed is None or fixed - lag >= 2:
                                    act.wait_ge(s_hT, QT * (c - lag - 1))
                                nc.scalar.activation(heads[:, (par + lag) % 2, g], bank_av[:, 0:T],
                                                     ACT.Copy).then_inc(s_ho, 1)
                            k = h - ST_LAG
                            lag, hh = -(k // HEADS), k % HEADS
                            if live(fixed, lag):
                                n = (c - lag) * HEADS + hh
                                act.wait_ge(s_ST, n + 1)
                                if fixed is None or fixed - lag >= 1:
                                    act.wait_ge(s_av, n - HEADS + 1)
                                nc.scalar.activation(probs[:, hh], bank_st(hh)[:, 0:2 * BAND], ACT.Exp,
                                                     scale=DH ** -0.5).then_inc(s_P, 1)
                            for t, at in ((0, 4), (1, 8)):
                                if h == at and live(fixed, -1):
                                    act.wait_ge(s_inT, 2 * (c + 1) + t + 1)
                                    if fixed is None or fixed >= 0:
                                        act.wait_ge(s_sto, 16 * (2 * c + t + 1))
                                    nc.scalar.activation(parts[:, t, 0], bank_in.rearrange("p (a t) -> p a t", a=DT),
                                                         ACT.Copy).then_inc(s_p1, 1)
                                if h == at + 1 and live(fixed, -1):
                                    act.wait_ge(s_r1, 2 * (c + 1) + t + 1)
                                    nc.scalar.activation(parts[:, t, 1], rest[:, t], ACT.Copy).then_inc(s_p2, 1)
                            if h == 2 and live(fixed, -1):
                                o = 1 - par
                                act.wait_ge(s_ctx[o], 8 * (c + 1 - o) + 16)
                                if fixed is None or fixed >= 0:
                                    act.wait_ge(s_inT, 2 * (c + 1))
                                nc.scalar.activation(cn[:].rearrange("p q (d h) -> p q h d", d=DH),
                                                     ctxs[:, o].rearrange("p q (h d) -> p q h d", d=DH),
                                                     ACT.Copy).then_inc(s_cn, 1)
                            if h == 6 and live(fixed, 0):
                                act.wait_ge(s_ctx[par], 8 * (c - par) + 16)
                                if fixed is None or fixed >= 2:
                                    act.wait_ge(s_av, (c - 1) * HEADS)
                                nc.scalar.activation(vals[:, par, :, :, 0:DH],
                                                     ctxs[:, par].rearrange("p q (h d) -> p q h d", d=DH),
                                                     ACT.Copy).then_inc(s_v, 1)
                            if h == 8 and (fixed is None or 0 <= fixed < B - 2):
                                act.wait_ge(s_v, c + 1)
                                act.dma_start(ctxs[:, par], ctx_in[c + 2].rearrange("(q p) d -> p q d", p=P)
                                              ).then_inc(s_ctx[par], 16)
                            for q, at in ((0, 8), (1, 14)):
                                if h == at and live(fixed, 2):
                                    act.wait_ge(s_yT, (c - 2) * QT + q + 1)
                                    nc.scalar.activation(yT[:], bank_y[:, 0:D].rearrange("p (a q) -> p a q", a=DT),
                                                         ACT.Copy).then_inc(s_yc, 1)

                    both(body, act.Fori)

                @block.vector
                def _(dve):
                    nc.vector.memset(K6[ROWS:P], 1.0).then_inc(s_ones, 1)
                    for i in range(NT):
                        if i % (XL * QT) == 0:
                            dve.wait_ge(s_x[i // (XL * QT)], 16)
                        nc.vector.bn_stats(st1[:, i, :], X[:, i, :]).then_inc(s_st, 1)
                    for i in range(NT):
                        dve.wait_ge(s_st, NT)
                        nc.vector.bn_aggr(mv1[:, i, :], st1[:, i, :]).then_inc(s_st, 1)
                    for i in range(10):
                        dve.wait_ge(s_wt, i + 1)
                        src = psum[:, i % 2, :]
                        if i < 9:
                            kind, j = divmod(i, 3)
                            if kind < 2:
                                dst = (wgT, wuT)[kind][:, :, 2 * P * j:2 * P * (j + 1)]
                                s = src.rearrange("p (a n) -> p a n", a=DT)
                            else:
                                dst = wdT[:, 2 * j:2 * j + 2, :]
                                s = src.rearrange("p (j n) -> p j n", j=2)
                        else:
                            dst, s = wpT[:], src.rearrange("p (a n) -> p a n", a=DT)
                        nc.vector.tensor_copy(dst, s).then_inc(s_wc, 1)
                    dve.wait_ge(s_std, 1)
                    nc.vector.reciprocal(rstd1[:], std1[:]).then_inc(s_rstd, 1)

                    def body(c, par, fixed):
                        for h in range(HEADS):
                            if h == 0 and live(fixed, -1):
                                if fixed is None or fixed >= 0:
                                    dve.wait_ge(s_inT, 2 * c + 1)
                                else:
                                    dve.wait_ge(s_rstd, 1)
                                for q in range(QT):
                                    i = (c + 1) * QT + q
                                    nc.vector.tensor_scalar(
                                        xn[:, q, :].rearrange("p (d h) -> p h d", d=DH),
                                        tile(X, i).rearrange("p (h d) -> p h d", d=DH), one(mv1, i, 0), col(rstd1, i),
                                        ALU.subtract, ALU.mult).then_inc(s_norm, 1)
                            if live(fixed, 0):
                                dve.wait_ge(s_S, c * HEADS + h + 1)
                                nc.vector.tensor_reduce(
                                    out=maxs[:, par, :, h], in_=bank_s(h)[:, 0:2 * BAND].rearrange("p (q k) -> p q k", q=QT),
                                    op=ALU.max, axis=AX_X).then_inc(s_max, 1)
                                if h % GROUP == GROUP - 1:
                                    g = h // GROUP
                                    m = maxs[:, par, :, GROUP * g:GROUP * (g + 1)]
                                    dve.wait_ge(s_max, c * HEADS + h + 1)
                                    if fixed is None or fixed >= 1:
                                        dve.wait_ge(s_nT, (c - 1) * NG + g + 1)
                                    nc.vector.tensor_scalar(neg[:, g, :, 0, :], m, -1.0, None,
                                                            ALU.mult).then_inc(s_n1, 1)
                                    dve.wait_ge(s_n1, c * NG + g + 1)
                                    nc.vector.scalar_tensor_tensor(
                                        out=neg[:, g, :, 1, :], in0=m, scalar=-1.0, in1=neg[:, g, :, 0, :],
                                        op0=ALU.mult, op1=ALU.subtract).then_inc(s_n2, 1)
                            if h % GROUP == 2:
                                lag, g = (1, 3) if h == 2 else (0, h // GROUP - 1)
                                if live(fixed, lag):
                                    dve.wait_ge(s_nT, (c - lag) * NG + g + 1)
                                    if fixed is None or fixed - lag >= 1:
                                        dve.wait_ge(s_sh[g % 2], 16 * (2 * (c - lag - 1) + g // 2 + 1))
                                    nc.vector.tensor_copy(negT[:, g, :], bank_neg).then_inc(s_nr, 1)
                            for t, at in ((0, 4), (1, 8)):
                                if h == at and live(fixed, -1):
                                    dve.wait_ge(s_p1, 2 * (c + 1) + t + 1)
                                    if fixed is None or fixed >= 0:
                                        dve.wait_ge(s_p3, 2 * c + t + 1)
                                    nc.vector.tensor_tensor(rest[:, t], bank_in.rearrange("p (a t) -> p a t", a=DT),
                                                            parts[:, t, 0], ALU.subtract).then_inc(s_r1, 1)
                            if h == 12 and live(fixed, 0):
                                for q in range(QT):
                                    i = c * QT + q
                                    nc.vector.tensor_tensor(tile(X, i), tile(X, i), bias[:],
                                                            ALU.add).then_inc(s_bx, 1)
                            for q, at in ((0, 6), (1, 12)):
                                if h == at and live(fixed, 2):
                                    n = (c - 2) * QT + q
                                    v = bank_y.rearrange("p (h w) -> p h w", w=VW)
                                    dve.wait_ge(s_hT, n + 1)
                                    nc.vector.reciprocal(inv[:].unsqueeze(2), v[:, :, DH:DH + 1]).then_inc(s_inv, 1)
                                    dve.wait_ge(s_inv, n + 1)
                                    if fixed != 2 or q > 0:
                                        dve.wait_ge(s_yT, n)
                                    nc.vector.tensor_tensor(y[:], v[:, :, 0:DH], inv[:].unsqueeze(2).to_broadcast([P, HEADS, DH]),
                                                            ALU.mult).then_inc(s_y, 1)
                            for q, at, lag in ((0, 10, 2), (1, 15, 2)):
                                if h == at and live(fixed, lag):
                                    n = (c - lag) * QT + q
                                    dve.wait_ge(s_pr, n + 1)
                                    dve.wait_ge(s_bx, n + 1)
                                    nc.vector.tensor_tensor(tile(X, n), bank_y[:, 0:D], tile(X, n),
                                                            ALU.add).then_inc(s_x1, 1)
                                    wait_apart(dve, s_x1, n + 1, s_wdve)
                                    nc.vector.bn_stats(st2[:], tile(X, n)).then_inc(s_st2, 1)
                                    wait_apart(dve, s_st2, n + 1, s_wdve)
                                    nc.vector.bn_aggr(mvq[:], st2[:]).then_inc(s_mv2, 1)
                                    dve.wait_ge(s_mv2, n + 1)
                                    nc.vector.tensor_scalar(tile(mv2, n), mvq[:], 1.0, None, ALU.mult)

                    both(body, dve.Fori)

                @block.tensor
                def _(pe):
                    pe.wait_ge(s_const, 7)
                    pe.wait_ge(s_wf, 3)
                    for i in range(10):
                        if i >= 2:
                            pe.wait_ge(s_wc, i - 1)
                        o = psum[:, i % 2, :]
                        kind, j = divmod(i, 3)
                        for u in range(2):
                            for v in range(2):
                                if kind < 2:
                                    w = wraw[:, kind].bitcast(F32).rearrange("p (j d) -> p j d", d=D)
                                    src = w[:, 2 * j + v, u * P:(u + 1) * P]
                                elif kind == 2:
                                    w = wraw[:, 2].bitcast(F32).rearrange("p (a d) -> p a d", d=HID)
                                    src = w[:, v, (2 * j + u) * P:(2 * j + u + 1) * P]
                                else:
                                    src = wpraw[:, v, u * P:(u + 1) * P]
                                last = nc.tensor.transpose(o[:, (2 * u + v) * P:(2 * u + v + 1) * P], src, ident[:])
                        last.then_inc(s_wt, 1)
                    pe.wait_ge(s_wc, 10)
                    pe.wait_ge(s_const, 11)
                    pe.wait_ge(s_ones, 1)

                    def body(c, par, fixed):
                        for h in range(HEADS):
                            if live(fixed, 0):
                                if h % HALF == 0:
                                    pe.wait_ge(s_op[h // HALF], 16 * LOADS * (c + 1))
                                n = c * HEADS + h
                                if fixed != 0 or h >= NS:
                                    pe.wait_ge(s_max, n - NS + 1)
                                o = bank_s(h)
                                nc.tensor.matmul(o[:, 0:2 * BAND], identb[:], maskb[:], start=True, stop=False,
                                                 skip_group_check=True)
                                for q in range(QT):
                                    last = nc.tensor.matmul(
                                        o[:, q * BAND:(q + 1) * BAND], Q6[0:ROWS, par, h, q * P:(q + 1) * P],
                                        K6[0:ROWS, par, h, q * WINDOW:q * WINDOW + BAND],
                                        start=False, stop=q == QT - 1, skip_group_check=True)
                                last.then_inc(s_S, 1)
                            k = h - ST_LAG
                            lag, hh = -(k // HEADS), k % HEADS
                            if live(fixed, lag):
                                p, n = (par + lag) % 2, (c - lag) * HEADS + hh
                                if hh % GROUP == 0:
                                    g = hh // GROUP
                                    pe.wait_ge(s_sh[g % 2], 16 * (2 * (c - lag) + g // 2 + 1))
                                if hh >= NST:
                                    pe.wait_ge(s_P, n - NST + 1)
                                elif fixed is None or fixed - lag >= 1:
                                    back = next(i for i in range(HEADS) if (HEADS - 1 - i) % NST == hh)
                                    pe.wait_ge(s_P, n - hh - back)
                                o = bank_st(hh)
                                for q in range(QT):
                                    last = nc.tensor.matmul(
                                        o[:, q * BAND:(q + 1) * BAND], K6[0:ALLROWS, p, hh, q * P:(q + 1) * P],
                                        Q6[0:ALLROWS, p, hh, q * WINDOW:q * WINDOW + BAND],
                                        start=True, stop=True)
                                last.then_inc(s_ST, 1)
                            k = h - AV_LAG
                            lag, hh = -(k // HEADS), k % HEADS
                            if live(fixed, lag):
                                p, g, r = (par + lag) % 2, hh // GROUP, hh % GROUP
                                if r == 0:
                                    pe.wait_ge(s_mk, GROUP * (NG * (c - lag) + g + 1))
                                    if g > 0 or fixed is None or fixed - lag >= 1:
                                        pe.wait_ge(s_ho, NG * (c - lag) + g)
                                    if g == 0:
                                        pe.wait_ge(s_v, c - lag + 1)
                                for q in range(QT):
                                    last = nc.tensor.matmul(
                                        bank_av[VW * r:VW * (r + 1), q * WINDOW:q * WINDOW + BAND],
                                        vals[:, p, q, hh, :], probs[:, hh, q * BAND:(q + 1) * BAND],
                                        start=q == 0, stop=q == QT - 1, skip_group_check=True)
                                last.then_inc(s_av, 1)
                            if h % GROUP == 1:
                                lag, g = (1, 3) if h == 1 else (0, h // GROUP - 1)
                                if live(fixed, lag):
                                    pe.wait_ge(s_n2, (c - lag) * NG + g + 1)
                                    if fixed is None or fixed >= 1 or g >= 1:
                                        pe.wait_ge(s_nr, (c - lag) * NG + g)
                                    if fixed is None:
                                        if h == 1:
                                            pe.wait_ge(s_r1, 2 * (c + 1))
                                        elif h == 5:
                                            pe.wait_ge(s_r1, 2 * (c + 1) + 1)
                                        elif h == 9:
                                            pe.wait_ge(s_r1, 2 * (c + 1) + 2)
                                    else:
                                        pe.wait_ge(s_r1, min(2 * B, 2 * (c + 1) + {1: 0, 5: 1, 9: 2, 13: 2}[h]))
                                    for q in range(QT):
                                        last = nc.tensor.transpose(
                                            bank_neg[:, q * P:(q + 1) * P],
                                            neg[:, g, q].rearrange("p s h -> p (s h)"), identb[:])
                                    last.then_inc(s_nT, 1)
                            for t, at in ((0, 3), (1, 7)):
                                if h == at and live(fixed, -1):
                                    if t == 0:
                                        pe.wait_ge(s_norm, QT * (c + 2))
                                        src = xn[:]
                                    else:
                                        pe.wait_ge(s_cn, c + 2)
                                        src = cn[:]
                                    if fixed is None or fixed >= 0 or t == 1:
                                        pe.wait_ge(s_r1, 2 * (c + 1) + t)
                                    if t == 0 and (fixed is None or fixed >= 1):
                                        pe.wait_ge(s_nr, c * NG)
                                    if t == 1 and (fixed is None or fixed >= 0):
                                        pe.wait_ge(s_nr, c * NG + 1)
                                    for u in range(DT):
                                        for q in range(QT):
                                            last = nc.tensor.transpose(
                                                bank_in[:, (u * QT + q) * P:(u * QT + q + 1) * P],
                                                src[:, q, u * P:(u + 1) * P], ident[:])
                                    last.then_inc(s_inT, 1)
                            for q, at in ((0, 5), (1, 11)):
                                n = (c - 2) * QT + q
                                if not live(fixed, 2):
                                    continue
                                if h == at:
                                    if q == 0:
                                        pe.wait_ge(s_ho, NG * (c - 1))
                                    if fixed != 2 or q > 0:
                                        pe.wait_ge(s_x1, n)
                                    for g in range(NG):
                                        last = nc.tensor.transpose(bank_y[:, g * P:(g + 1) * P],
                                                                   heads[:, par, g, q * P:(q + 1) * P], ident[:])
                                    last.then_inc(s_hT, 1)
                                if h == at + 2:
                                    pe.wait_ge(s_y, n + 1)
                                    for u in range(DT):
                                        last = nc.tensor.transpose(
                                            bank_y[:, u * P:(u + 1) * P],
                                            y[:].rearrange("p h d -> p (h d)")[:, u * P:(u + 1) * P], ident[:])
                                    last.then_inc(s_yT, 1)
                                if h == at + 4:
                                    pe.wait_ge(s_yc, n + 1)
                                    for u in range(DT):
                                        last = nc.tensor.matmul(bank_y[:, 0:D], yT[:, u, :], wpT[:, u, :],
                                                                start=u == 0, stop=u == DT - 1)
                                    last.then_inc(s_pr, 1)

                    both(body, pe.Fori)

        with ExitStack() as f:
            CH = 4
            TOK = CH * P
            NC = NT // CH
            std2 = sb("std2", [P, NT], F32, f)
            xn2 = sb("xn2", [P, CH, D], F32, f)
            xh = sb("xh", [P, 2, DT, TOK], F16, f)
            xl = sb("xl", [P, 2, DT, TOK], F16, f)
            gs = sb("gs", [P, 2, TOK], F32, f)
            hf = sb("hf", [P, 2, TOK], F32, f)
            hh_ = sb("hh", [P, 2, HT, TOK], F32R, f)
            hl_ = sb("hl", [P, 2, HT, TOK], F32R, f)
            yo = sb("yo", [P, CH, D], F32, f)

            t_std = sem("std2_done", f)
            t_wsp = sem("waits2_of_sp", f)
            t_rs = sem("rstd2_done", f)
            t_n = sem("normed2", f)
            t_xT = sem("x2_transposed", f)
            t_xh = sem("x2_high_done", f)
            t_xl = sem("x2_low_done", f)
            t_g = sem("gate_ready", f)
            t_u = sem("up_ready", f)
            t_gs = sem("silu_done", f)
            t_h = sem("hidden_done", f)
            t_hh = sem("hidden_high_done", f)
            t_hl = sem("hidden_low_done", f)
            t_d = sem("down_ready", f)
            t_y = sem("y_done", f)
            t_o = [sem(f"y_stored{i}", f) for i in range(CH)]

            bx = psum[:, 0:2, :]

            def bg(j):
                return psum[:, 2 + j % 2, :]

            def bu(j):
                return psum[:, 4 + j % 2, :]

            def bd(t):
                return psum[:, 6 + t // 2, (t % 2) * D:(t % 2 + 1) * D]

            def chunks(body, fori):
                first, last = 2, 2 + 2 * ((NC - 1 - 2) // 2)
                for c in range(-1, first):
                    body(c, c % 2, c)
                with fori(first, last - 1, 2) as c:
                    body(c, 0, None)
                    body(c + 1, 1, None)
                for c in range(last, NC + 1):
                    body(c, c % 2, c)

            def on(fixed, lag):
                return fixed is None or 0 <= fixed - lag < NC

            with nc.Block() as block:

                @block.scalar
                def _(act):
                    nc.scalar.activation(std2[:], mv2[:, :, 1], ACT.Sqrt, bias=eps[:]).then_inc(t_std, 1)

                    def body(c, par, fixed):
                        for j in range(HT):
                            if on(fixed, 0):
                                n = c * HT + j
                                act.wait_ge(t_g, n + 1)
                                if fixed != 0 or j >= 2:
                                    act.wait_ge(t_h, n - 1)
                                nc.scalar.activation(gs[:, j % 2], bg(j), ACT.Silu, scale=WSCALE).then_inc(t_gs, 1)
                                act.wait_ge(t_h, n + 1)
                                if j == 0 and (fixed is None or fixed >= 2):
                                    act.wait_ge(t_d, CH * (c - 1))
                                nc.scalar.activation(hh_[:, par, j], hf[:, j % 2], ACT.Copy).then_inc(t_hh, 1)
                            if j == 3 and on(fixed, -1):
                                act.wait_ge(t_xT, c + 2)
                                if fixed is None or fixed >= 1:
                                    act.wait_ge(t_u, HT * c)
                                nc.scalar.activation(xh[:, 1 - par], bx, ACT.Copy).then_inc(t_xh, 1)

                    chunks(body, act.Fori)

                @block.gpsimd
                def _(pool):
                    def body(c, par, fixed):
                        for j in range(HT):
                            if on(fixed, 0):
                                pool.wait_ge(t_hh, c * HT + j + 1)
                                nc.gpsimd.tensor_tensor(hl_[:, par, j], hf[:, j % 2], hh_[:, par, j].bitcast(F32),
                                                        ALU.subtract).then_inc(t_hl, 1)

                    chunks(body, pool.Fori)

                @block.vector
                def _(dve):
                    dve.wait_ge(t_std, 1)
                    nc.vector.reciprocal(rstd2[:], std2[:]).then_inc(t_rs, 1)
                    dve.wait_ge(t_rs, 1)

                    def body(c, par, fixed):
                        for j in range(HT):
                            if j == 0 and on(fixed, -1):
                                if fixed is None or fixed >= 0:
                                    dve.wait_ge(t_xT, c + 1)
                                for t in range(CH):
                                    i = (c + 1) * CH + t
                                    nc.vector.tensor_scalar(xn2[:, t, :], tile(X, i), one(mv2, i, 0), col(rstd2, i),
                                                            ALU.subtract, ALU.mult).then_inc(t_n, 1)
                            if on(fixed, 0):
                                n = c * HT + j
                                dve.wait_ge(t_gs, n + 1)
                                dve.wait_ge(t_u, n + 1)
                                if fixed != 0 or j >= 2:
                                    dve.wait_ge(t_hl, n - 1)
                                nc.vector.tensor_tensor(hf[:, j % 2], gs[:, j % 2], bu(j), ALU.mult).then_inc(t_h, 1)
                            if j == 3 and on(fixed, -1):
                                dve.wait_ge(t_xh, c + 2)
                                nc.vector.tensor_tensor(xl[:, 1 - par], bx, xh[:, 1 - par], ALU.subtract).then_inc(t_xl, 1)
                            if 1 <= j <= CH and on(fixed, 1):
                                t = j - 1
                                i = (c - 1) * CH + t
                                dve.wait_ge(t_d, i + 1)
                                if fixed is None or fixed >= 2:
                                    dve.wait_ge(t_o[t], 16 * (c - 1))
                                nc.vector.scalar_tensor_tensor(
                                    out=yo[:, t, :], in0=bd(t), scalar=WSCALE * WSCALE, in1=tile(X, i),
                                    op0=ALU.mult, op1=ALU.add).then_inc(t_y, 1)

                    chunks(body, dve.Fori)

                @block.sync
                def _(sp):
                    flat = out.rearrange("b (q p) d -> (b q) p d", p=P)

                    def body(c, par, fixed):
                        if on(fixed, 1):
                            for t in range(CH):
                                i = (c - 1) * CH + t
                                wait_apart(sp, t_y, i + 1, t_wsp)
                                dst = flat[i] if isinstance(i, int) else flat[bass.ds(i, 1)].rearrange("a p d -> (a p) d")
                                sp.dma_start(dst, yo[:, t, :]).then_inc(t_o[t], 16)

                    chunks(body, sp.Fori)
                    for t in range(CH):
                        sp.wait_ge(t_o[t], 16 * NC)

                @block.tensor
                def _(pe):
                    def body(c, par, fixed):
                        for j in range(HT):
                            if on(fixed, 0):
                                n = c * HT + j
                                if j == 0:
                                    pe.wait_ge(t_xl, c + 1)
                                for w, o, ready, free in ((wgT, bg(j), t_g, t_gs), (wuT, bu(j), t_u, t_h)):
                                    if fixed != 0 or j >= 2:
                                        pe.wait_ge(free, n - 1)
                                    for u in range(DT):
                                        for v, xx in enumerate((xh, xl)):
                                            last = nc.tensor.matmul(o, w[:, u, j * P:(j + 1) * P], xx[:, par, u, :],
                                                                    start=u == 0 and v == 0, stop=u == DT - 1 and v == 1)
                                    last.then_inc(ready, 1)
                            if j == 1 and on(fixed, -1):
                                pe.wait_ge(t_n, CH * (c + 2))
                                if fixed is None or fixed >= 0:
                                    pe.wait_ge(t_xl, c + 1)
                                for u in range(DT):
                                    for t in range(CH):
                                        last = nc.tensor.transpose(bx[:, u, t * P:(t + 1) * P],
                                                                   xn2[:, t, u * P:(u + 1) * P], ident[:])
                                last.then_inc(t_xT, 1)
                            if j < CH and on(fixed, 1):
                                t = j
                                if j == 0:
                                    pe.wait_ge(t_hl, HT * c)
                                    pe.wait_ge(t_hh, HT * c)
                                if fixed is None or fixed >= 2:
                                    pe.wait_ge(t_y, CH * (c - 2) + 2 * (t // 2) + 2)
                                if t % 2:
                                    pe.wait_ge(t_y, CH * (c - 1) + t)
                                for k in range(HT):
                                    for v, m in enumerate((hh_, hl_)):
                                        last = nc.tensor.matmul(bd(t), m[:, 1 - par, k, t * P:(t + 1) * P], wdT[:, k, :],
                                                                start=k == 0 and v == 0, stop=k == HT - 1 and v == 1)
                                last.then_inc(t_d, 1)

                    chunks(body, pe.Fori)


_INS = ['x', 'ctx_1024', 'L0_xattn_W_proj', 'L0_xattn_b_proj', 'L0_ffn_w_gate', 'L0_ffn_w_up', 'L0_ffn_w_down']


def kernel(**inputs):
    import numpy as np
    import concourse.bacc as bacc
    from concourse.bass_utils import run_bass_kernel_spmd

    nc = bacc.Bacc("TRN2", target_bir_lowering=False, num_devices=1)
    arrays, args = {}, []
    for name in _INS:
        a = np.ascontiguousarray(inputs[name])
        arrays[f"in_{name}"] = a
        args.append(nc.dram_tensor(f"in_{name}", a.shape, mybir.dt.from_np(a.dtype), kind="ExternalInput").ap())
    args.append(nc.dram_tensor("out_0", inputs["x"].shape, F32, kind="ExternalOutput").ap())
    block_kernel(nc, *args)
    r = run_bass_kernel_spmd(nc, [arrays], core_ids=[0])
    return r.results[0]["out_0"]
```

```python
from contextlib import ExitStack

import concourse.bass as bass
from concourse import mybir

F32 = mybir.dt.float32
F32R = mybir.dt.float32r
F16 = mybir.dt.float16
BF16 = mybir.dt.bfloat16
I32 = mybir.dt.int32
ALU = mybir.AluOpType
ACT = mybir.ActivationFunctionType
AX_X = mybir.AxisListType.X

P = 128


def block_kernel(nc, x_in, ctx_in, w_proj, b_proj, w_gate, w_up, w_down, out):
    B, T, D = x_in.shape
    HID = w_gate.shape[0]
    HEADS, WINDOW = 16, 64
    DH = D // HEADS
    QT = T // P
    DT = D // P
    HT = HID // P
    NT = B * QT
    BAND = P + WINDOW
    EPS = 1e-5
    WSCALE = 1.0 / 127.0
    assert T == 2 * P and D == 2 * P and WINDOW == P // 2 and DH == 16

    ROWS = 6 * DH
    SHIFT = ROWS
    ALLROWS = ROWS + 2
    GROUP = 4
    NG = HEADS // GROUP
    VW = 32
    HALF = HEADS // 2
    LOADS = 6
    ST_LAG = 12
    NS, NST = 2, 3

    def tile(m, i):
        return m[:, i, :] if isinstance(i, int) else m[:, bass.ds(i, 1), :].rearrange("p a d -> p (a d)")

    def one(m, i, k):
        return m[:, i, k:k + 1] if isinstance(i, int) else m[:, bass.ds(i, 1), k:k + 1].rearrange("p a d -> p (a d)")

    def col(m, i):
        return m[:, i:i + 1] if isinstance(i, int) else m[:, bass.ds(i, 1)]

    def wait_apart(engine, semaphore, value, counter):
        engine.wait_ge(semaphore, value)
        engine.sem_inc(counter, 1)

    ctx = ExitStack()
    with ctx:
        def sb(name, shape, dt, stack=ctx):
            return stack.enter_context(nc.sbuf_tensor(name, shape, dt))

        def sem(name, stack=ctx):
            return stack.enter_context(nc.semaphore(name))

        psum = ctx.enter_context(nc.psum_tensor("psum", [P, 8, 512], F32))

        X = sb("X", [P, NT, D], F32)
        ident = sb("ident", [P, P], F32)
        wgT = sb("wgT", [P, DT, HID], F16)
        wuT = sb("wuT", [P, DT, HID], F16)
        wdT = sb("wdT", [P, HT, D], F32R)
        mv2 = sb("mv2", [P, NT, 2], F32)
        rstd2 = sb("rstd2", [P, NT], F32)
        eps = sb("eps", [P, 1], F32)

        with ExitStack() as a:
            ctxs = sb("ctxs", [P, 2, QT, D], F32, a)
            Q6 = sb("Q6", [P, 2, HEADS, T], BF16, a)
            K6 = sb("K6", [P, 2, HEADS, T], BF16, a)
            probs = sb("probs", [P, HEADS, 2 * BAND], F32, a)
            vals = sb("vals", [P, 2, QT, HEADS, VW], F32, a)
            identb = sb("identb", [P, P], BF16, a)
            maskb = sb("maskb", [P, 2 * BAND], BF16, a)
            wraw = sb("wraw", [P, 3, HT * D], I32, a)
            wpraw = sb("wpraw", [P, DT, D], F32, a)
            wpT = sb("wpT", [P, DT, D], F32, a)
            bias = sb("bias", [P, D], F32, a)
            st1 = sb("st1", [P, NT, 6], F32, a)
            mv1 = sb("mv1", [P, NT, 2], F32, a)
            std1 = sb("std1", [P, NT], F32, a)
            nmr1 = sb("nmr1", [P, NT], F32, a)
            rstd1 = sb("rstd1", [P, NT], F32, a)
            st2 = sb("st2", [P, 6], F32, a)
            mvq = sb("mvq", [P, 2], F32, a)
            xn = sb("xn", [P, QT, D], F32, a)
            cn = sb("cn", [P, QT, D], F32, a)
            parts = sb("parts", [P, 2, 3, DT, T], BF16, a)
            rest = sb("rest", [P, 2, DT, T], F32, a)
            maxs = sb("maxs", [P, 2, QT, HEADS], F32, a)
            neg = sb("neg", [P, NG, QT, 2, GROUP], BF16, a)
            negT = sb("negT", [2 * GROUP, NG, T], BF16, a)
            heads = sb("heads", [P, 2, NG, T], F32, a)
            inv = sb("inv", [P, HEADS], F32, a)
            y = sb("y", [P, HEADS, DH], F32, a)
            yT = sb("yT", [P, DT, P], F32, a)
            scr = nc.dram_tensor("parts_scratch", [2, 2, 3, D, T], BF16, kind="Internal").ap()

            XL = 4
            s_x = [sem(f"x_loaded{i}", a) for i in range(B // XL)]
            s_w = [sem(f"{w}_loaded", a) for w in ("bias", "ffn_weights", "projection")]
            s_wpool, s_wsp, s_wdve, s_wact = (sem(f"waits_of_{e}", a) for e in ("pool", "sp", "dve", "act"))
            s_ctx = [sem(f"ctx_loaded{i}", a) for i in range(2)]
            s_const = sem("constants_ready", a)
            s_ones = sem("ones_rows_ready", a)
            s_wf = sem("weights_float", a)
            s_wt = sem("weights_transposed", a)
            s_wc = sem("weights_copied", a)
            s_st = sem("stats_done", a)
            s_ag = sem("stats_aggregated", a)
            s_std = sem("std_done", a)
            s_inv1 = sem("std_inverted", a)
            s_rstd = sem("rstd_done", a)
            s_norm = sem("normed", a)
            s_cn = sem("context_ordered", a)
            s_inT = sem("inputs_transposed", a)
            s_p1 = sem("part1_done", a)
            s_r1 = sem("rest1_done", a)
            s_p2 = sem("part2_done", a)
            s_p3 = sem("part3_done", a)
            s_sto = sem("parts_stored", a)
            s_op = [sem(f"operands_loaded{i}", a) for i in range(2)]
            s_S = sem("scores_ready", a)
            s_max = sem("max_done", a)
            s_n1 = sem("neg_high_done", a)
            s_n2 = sem("neg_low_done", a)
            s_nT = sem("neg_transposed", a)
            s_nr = sem("neg_rows_ready", a)
            s_sh = [sem(f"shift_landed{i}", a) for i in range(2)]
            s_ST = sem("scoresT_ready", a)
            s_P = sem("probs_ready", a)
            s_mk = sem("probs_masked", a)
            s_v = sem("vals_ready", a)
            s_av = sem("heads_summed", a)
            s_ho = sem("heads_copied", a)
            s_hT = sem("heads_transposed", a)
            s_inv = sem("sums_inverted", a)
            s_y = sem("y_ready", a)
            s_yT = sem("y_transposed", a)
            s_yc = sem("yT_copied", a)
            s_pr = sem("projected", a)
            s_x1 = sem("x1_ready", a)
            s_bx = sem("bias_added", a)
            s_st2 = sem("stats2_done", a)
            s_mv2 = sem("mv2_done", a)

            bank_in, bank_y, bank_av = psum[:, 5, :], psum[:, 6, :], psum[:, 7, :]

            bank_neg = bank_in.bitcast(BF16)[0:2 * GROUP, 0:T]

            def bank_s(h):
                return psum[:, h % NS, :]

            def bank_st(n):
                return psum[:, NS + n % NST, :]

            def x_rows(b0, nb):
                return x_in[b0:b0 + nb].rearrange("b (q p) d -> p (b q) d", p=P)

            def steps(body, fori):
                first, last = 4, 4 + 2 * ((B - 3 - 4) // 2)
                for c in range(-3, first):
                    yield c
                    body(c, c % 2, c)
                with fori(first, last - 1, 2) as c:
                    body(c, 0, None)
                    body(c + 1, 1, None)
                for c in range(last, B + 3):
                    yield c
                    body(c, c % 2, c)

            def live(fixed, lag):
                return fixed is None or 0 <= fixed - lag < B

            def later(fixed, lag, n):
                return fixed is None or fixed - lag >= n

            EARLY = 4 * QT
            MIDDLE = 8 * QT

            with nc.Block() as block:

                @block.gpsimd
                def _(pool):
                    nc.gpsimd.memset(ident[:], 0.0).then_inc(s_const, 1)
                    nc.gpsimd.memset(identb[:], 0.0).then_inc(s_const, 1)
                    nc.gpsimd.memset(maskb[:], 0.0).then_inc(s_const, 1)
                    nc.gpsimd.memset(vals[:], 1.0).then_inc(s_const, 1)
                    nc.gpsimd.memset(eps[:], EPS).then_inc(s_const, 1)
                    pool.wait_ge(s_const, 5)
                    for m in (ident, identb):
                        nc.gpsimd.affine_select(out=m[:], in_=m[:], compare_op=ALU.not_equal, fill=1.0,
                                                base=0, pattern=[[-1, P]], channel_multiplier=1).then_inc(s_const, 1)
                    for i, (t, base, step, cm) in enumerate([(0, WINDOW, -1, 1), (0, WINDOW, 1, -1),
                                                             (1, 0, 1, -1), (1, P, -1, 1)]):
                        m = maskb[:, t * BAND:(t + 1) * BAND]
                        pool.wait_ge(s_const, 7 + i)
                        nc.gpsimd.affine_select(out=m, in_=m, compare_op=ALU.is_ge, fill=-1e30, base=base,
                                                pattern=[[step, BAND]], channel_multiplier=cm).then_inc(s_const, 1)
                    pool.wait_ge(s_w[0], 16)

                    def body(c, par, fixed):
                        for h in range(HEADS):
                            if h % GROUP == 0 and live(fixed, 1):
                                g = h // GROUP
                                wait_apart(pool, s_P, (c - 1) * HEADS + GROUP * (g + 1), s_wpool)
                                for lo, n, base, step, cm in ((0, WINDOW, WINDOW, 1, -1),
                                                              (WINDOW, P, 0, -1, 1),
                                                              (BAND, P, 0, 1, -1),
                                                              (BAND + P, WINDOW, 0, -1, 1)):
                                    p = probs[:, GROUP * g:GROUP * (g + 1), lo:lo + n]
                                    nc.gpsimd.affine_select(
                                        out=p, in_=p, compare_op=ALU.is_ge, fill=0.0, base=base,
                                        pattern=[[0, GROUP], [step, n]], channel_multiplier=cm).then_inc(s_mk, 1)
                            for t, at, b in ((0, 15, 2), (1, 7, 1)):
                                if h == at and live(fixed, -b):
                                    pool.wait_ge(s_p2, 2 * (c + b) + t + 1)
                                    nc.gpsimd.tensor_tensor(parts[:, t, 2], rest[:, t], parts[:, t, 1],
                                                            ALU.subtract).then_inc(s_p3, 1)
                            if h == 12 and live(fixed, 0):
                                wait_apart(pool, s_norm, QT * (c + 1), s_wpool)
                                for q in range(QT):
                                    i = c * QT + q
                                    nc.gpsimd.tensor_tensor(tile(X, i), tile(X, i), bias[:], ALU.add).then_inc(s_bx, 1)

                    for c in steps(body, pool.Fori):
                        pass

                @block.sync
                def _(sp):
                    for b0 in range(0, B, XL):
                        sp.dma_start(X[:, b0 * QT:(b0 + XL) * QT, :], x_rows(b0, XL)).then_inc(s_x[b0 // XL], 16)
                    for i, w in enumerate((w_gate, w_up)):
                        sp.dma_start(wraw[:, i].rearrange("p (a d) -> p a d", d=D),
                                     w.rearrange("(a p) d -> p a d", p=P)).then_inc(s_w[1], 16)
                    sp.dma_start(wraw[:, 2].rearrange("p (a d) -> p a d", d=HID),
                                 w_down.rearrange("(a p) d -> p a d", p=P)).then_inc(s_w[1], 16)

                    def shift(c, par, fixed, g, lag):
                        if live(fixed, lag):
                            p = (par + lag) % 2
                            sp.wait_ge(s_nr, (c - lag) * NG + g + 1)
                            sp.dma_start(Q6[SHIFT:ALLROWS, p, GROUP * g:GROUP * (g + 1), :],
                                         negT[:, g, :]).then_inc(s_sh[g % 2], 16)

                    def store(c, par, fixed, t):
                        b = (2, 1)[t]
                        if live(fixed, -b):
                            sp.wait_ge(s_p3, 2 * (c + b) + t + 1)
                            sp.dma_start(scr[t, (par + b) % 2].rearrange("s (a p) t -> p (s a) t", p=P),
                                         parts[:, t].rearrange("p s a t -> p (s a) t")).then_inc(s_sto, 16)

                    def load(c, par, fixed, half, t):
                        hs = slice(half * HALF, (half + 1) * HALF)
                        if not live(fixed, -1):
                            return
                        o = 1 - par
                        if t == 0 and later(fixed, -1, 2):
                            wait_apart(sp, s_ST, (c - 1) * HEADS + (half + 1) * HALF, s_wsp)
                        elif t == 0 and fixed == 0:
                            sp.wait_ge(s_S, half * HALF + 1)
                        if half == 0:
                            sp.wait_ge(s_sto, 16 * (2 * (c + 1) + t + 1))

                        def rows(s, n):
                            if t == 0:
                                v = scr[t, o, s].rearrange("(d h) t -> d h t", h=HEADS)[:, hs, :]
                                v = v.rearrange("d h t -> d (h t)")
                                return bass.AP(tensor=v.tensor, offset=v.offset, ap=[[0, n]] + [list(z) for z in v.ap])
                            v = scr[t, o, s:s + n].rearrange("s (d h) t -> (s d) h t", h=HEADS)
                            return v[:, hs, :].rearrange("p h t -> p (h t)")
                        for slot, s, n in (((0, 0, 3), (3, 1, 2), (5, 2, 1)), ((0, 0, 3), (3, 0, 2), (5, 0, 1)))[t]:
                            sp.dma_start((Q6, K6)[t][slot * DH:(slot + n) * DH, o, hs, :].rearrange("p h t -> p (h t)"),
                                         rows(s, n)).then_inc(s_op[half], 16)

                    def body(c, par, fixed):
                        shift(c, par, fixed, 3, 1)
                        load(c, par, fixed, 0, 0)
                        shift(c, par, fixed, 0, 0)
                        store(c, par, fixed, 1)
                        load(c, par, fixed, 0, 1)
                        shift(c, par, fixed, 1, 0)
                        load(c, par, fixed, 1, 0)
                        load(c, par, fixed, 1, 1)
                        shift(c, par, fixed, 2, 0)
                        store(c, par, fixed, 0)

                    for c in steps(body, sp.Fori):
                        pass

                @block.scalar
                def _(act):
                    for i in range(2):
                        act.dma_start(ctxs[:, i], ctx_in[i].rearrange("(q p) d -> p q d", p=P)).then_inc(s_ctx[i], 16)
                    act.dma_start(bias[:], b_proj.partition_broadcast(P)).then_inc(s_w[0], 16)
                    act.dma_start(wpraw[:], w_proj.rearrange("(a p) d -> p a d", p=P)).then_inc(s_w[2], 16)

                    def std(lo, hi, n):
                        act.wait_ge(s_ag, hi)
                        nc.scalar.activation(std1[:, lo:hi], mv1[:, lo:hi, 1], ACT.Sqrt, bias=eps[:]).then_inc(s_std, 1)

                    act.wait_ge(s_const, 5)
                    std(0, EARLY, 0)

                    def body(c, par, fixed):
                        for h in range(HEADS):
                            g = h // GROUP
                            if h % GROUP == 3:
                                lag, g1 = (1, 3) if h == 3 else (0, g - 1)
                                if live(fixed, lag):
                                    act.wait_ge(s_nT, (c - lag) * NG + g1 + 1)
                                    if later(fixed, lag, 1):
                                        act.wait_ge(s_sh[g1 % 2], 16 * (2 * (c - lag - 1) + g1 // 2 + 1))
                                    nc.scalar.activation(negT[:, g1, :], bank_neg, ACT.Copy).then_inc(s_nr, 1)
                            if h % GROUP == 0:
                                lag, g1 = (2, 3) if h == 0 else (1, g - 1)
                                if live(fixed, lag):
                                    act.wait_ge(s_av, (c - lag) * NG + g1 + 1)
                                    if later(fixed, lag, 2):
                                        act.wait_ge(s_hT, QT * (c - lag - 1))
                                    nc.scalar.activation(heads[:, (par + lag) % 2, g1], bank_av[:, 0:T],
                                                         ACT.Copy).then_inc(s_ho, 1)
                            for q, at in ((0, 5), (1, 13)):
                                if h == at and live(fixed, 2):
                                    act.wait_ge(s_yT, (c - 2) * QT + q + 1)
                                    nc.scalar.activation(yT[:], bank_y[:, 0:D].rearrange("p (a q) -> p a q", a=DT),
                                                         ACT.Copy).then_inc(s_yc, 1)
                            for t, at, b in ((0, 12, 2), (1, 4, 1)):
                                if h == at and live(fixed, -b):
                                    act.wait_ge(s_inT, 2 * (c + b) + t + 1)
                                    if later(fixed, -b, 1):
                                        act.wait_ge(s_sto, 16 * (2 * (c + b) + t - 1))
                                    nc.scalar.activation(parts[:, t, 0], bank_in.rearrange("p (a t) -> p a t", a=DT),
                                                         ACT.Copy).then_inc(s_p1, 1)
                            lag, hh = (1, h - ST_LAG + HEADS) if h < ST_LAG else (0, h - ST_LAG)
                            if live(fixed, lag):
                                n = (c - lag) * HEADS + hh
                                act.wait_ge(s_ST, n + 1)
                                if hh % GROUP == 0 and later(fixed, lag, 1):
                                    act.wait_ge(s_av, (c - lag - 1) * NG + hh // GROUP + 1)
                                nc.scalar.activation(probs[:, hh], bank_st(hh)[:, 0:2 * BAND], ACT.Exp,
                                                     scale=DH ** -0.5).then_inc(s_P, 1)
                            for t, at, b in ((0, 14, 2), (1, 6, 1)):
                                if h == at and live(fixed, -b):
                                    act.wait_ge(s_r1, 2 * (c + b) + t + 1)
                                    nc.scalar.activation(parts[:, t, 1], rest[:, t], ACT.Copy).then_inc(s_p2, 1)
                            if h == 1 and live(fixed, 0):
                                act.wait_ge(s_ctx[par], 8 * (c - par) + 16)
                                if later(fixed, 0, 2):
                                    act.wait_ge(s_av, (c - 1) * NG)
                                nc.scalar.activation(vals[:, par, :, :, 0:DH],
                                                     ctxs[:, par].rearrange("p q (h d) -> p q h d", d=DH),
                                                     ACT.Copy).then_inc(s_v, 1)
                            if h == 3 and (fixed is None or 0 <= fixed < B - 2):
                                act.wait_ge(s_v, c + 1)
                                act.dma_start(ctxs[:, par], ctx_in[c + 2].rearrange("(q p) d -> p q d", p=P)
                                              ).then_inc(s_ctx[par], 16)
                            if h == 14 and live(fixed, -3):
                                if later(fixed, -3, 1):
                                    wait_apart(act, s_inT, 2 * (c + 2) + 1, s_wact)
                                act.wait_ge(s_rstd, 1 if fixed is not None and fixed + 3 < EARLY // QT else 2)
                                for q in range(QT):
                                    i = (c + 3) * QT + q
                                    nc.scalar.activation(
                                        xn[:, q, :].rearrange("p (d h) -> p h d", d=DH),
                                        tile(X, i).rearrange("p (h d) -> p h d", d=DH), ACT.Identity,
                                        bias=col(nmr1, i), scale=col(rstd1, i)).then_inc(s_norm, 1)
                            if h == 10 and live(fixed, -2):
                                act.wait_ge(s_ctx[par], 8 * (c + 2 - par) + 16)
                                if fixed is None or fixed > -2:
                                    act.wait_ge(s_inT, 2 * (c + 2))
                                nc.scalar.activation(cn[:].rearrange("p q (d h) -> p q h d", d=DH),
                                                     ctxs[:, par].rearrange("p q (h d) -> p q h d", d=DH),
                                                     ACT.Copy).then_inc(s_cn, 1)
                    for c in steps(body, act.Fori):
                        if c == 0:
                            std(EARLY, NT, 1)
                        if c == 1:
                            act.wait_ge(s_w[1], 48)
                            for i in range(3):
                                nc.scalar.activation(wraw[:, i].bitcast(F32), wraw[:, i], ACT.Copy).then_inc(s_wf, 1)

                @block.vector
                def _(dve):
                    def stats(lo, hi):
                        for i in range(lo, hi):
                            if i % (XL * QT) == 0:
                                dve.wait_ge(s_x[i // (XL * QT)], 16)
                            nc.vector.bn_stats(st1[:, i, :], X[:, i, :]).then_inc(s_st, 1)
                        dve.wait_ge(s_st, hi)
                        for i in range(lo, hi):
                            nc.vector.bn_aggr(mv1[:, i, :], st1[:, i, :]).then_inc(s_ag, 1)

                    def invert(lo, hi, n):
                        dve.wait_ge(s_std, n)
                        nc.vector.reciprocal(rstd1[:, lo:hi], std1[:, lo:hi]).then_inc(s_inv1, 1)
                        dve.wait_ge(s_inv1, n)
                        nc.vector.scalar_tensor_tensor(out=nmr1[:, lo:hi], in0=mv1[:, lo:hi, 0], scalar=-1.0,
                                                       in1=rstd1[:, lo:hi], op0=ALU.mult, op1=ALU.mult).then_inc(s_rstd, 1)

                    stats(0, EARLY)
                    nc.vector.memset(K6[ROWS:P], 1.0).then_inc(s_ones, 1)
                    invert(0, EARLY, 1)

                    def body(c, par, fixed):
                        for h in range(HEADS):
                            g = h // GROUP
                            if h % GROUP in (0, 1):
                                lag, g1 = (1, 3) if h < 2 else (0, g - 1)
                                if live(fixed, lag):
                                    m = maxs[:, (par + lag) % 2, :, GROUP * g1:GROUP * (g1 + 1)]
                                    if h % GROUP == 0:
                                        dve.wait_ge(s_max, (c - lag) * HEADS + GROUP * (g1 + 1))
                                        if later(fixed, lag, 1):
                                            dve.wait_ge(s_nT, (c - lag - 1) * NG + g1 + 1)
                                        nc.vector.tensor_scalar(neg[:, g1, :, 0, :], m, -1.0, None,
                                                                ALU.mult).then_inc(s_n1, 1)
                                    else:
                                        dve.wait_ge(s_n1, (c - lag) * NG + g1 + 1)
                                        nc.vector.scalar_tensor_tensor(
                                            out=neg[:, g1, :, 1, :], in0=m, scalar=-1.0, in1=neg[:, g1, :, 0, :],
                                            op0=ALU.mult, op1=ALU.subtract).then_inc(s_n2, 1)
                            for t, at, b in ((0, 13, 2), (1, 5, 1)):
                                if h == at and live(fixed, -b):
                                    dve.wait_ge(s_p1, 2 * (c + b) + t + 1)
                                    if later(fixed, -b, 1):
                                        dve.wait_ge(s_p3, 2 * (c + b) + t - 1)
                                    nc.vector.tensor_tensor(rest[:, t], bank_in.rearrange("p (a t) -> p a t", a=DT),
                                                            parts[:, t, 0], ALU.subtract).then_inc(s_r1, 1)
                            for q, at in ((0, 2), (1, 10)):
                                n = (c - 2) * QT + q
                                if not live(fixed, 2):
                                    continue
                                v = bank_y.rearrange("p (h w) -> p h w", w=VW)
                                if h == at:
                                    dve.wait_ge(s_hT, n + 1)
                                    nc.vector.reciprocal(inv[:].unsqueeze(2), v[:, :, DH:DH + 1]).then_inc(s_inv, 1)
                                if h == at + 1:
                                    dve.wait_ge(s_inv, n + 1)
                                    if fixed != 2 or q > 0:
                                        dve.wait_ge(s_yT, n)
                                    nc.vector.tensor_tensor(y[:], v[:, :, 0:DH], inv[:].unsqueeze(2).to_broadcast([P, HEADS, DH]),
                                                            ALU.mult).then_inc(s_y, 1)
                            for q, at, lag in ((0, 8, 2), (1, 0, 3)):
                                n = (c - lag) * QT + q
                                if h == at and live(fixed, lag):
                                    dve.wait_ge(s_pr, n + 1)
                                    dve.wait_ge(s_bx, n + 1)
                                    nc.vector.tensor_tensor(tile(X, n), bank_y[:, 0:D], tile(X, n),
                                                            ALU.add).then_inc(s_x1, 1)
                            if live(fixed, 0):
                                dve.wait_ge(s_S, c * HEADS + h + 1)
                                nc.vector.tensor_reduce(
                                    out=maxs[:, par, :, h], in_=bank_s(h)[:, 0:2 * BAND].rearrange("p (q k) -> p q k", q=QT),
                                    op=ALU.max, axis=AX_X).then_inc(s_max, 1)
                            for q, at, lag in ((0, 8, 2), (1, 0, 3)):
                                n = (c - lag) * QT + q
                                if not live(fixed, lag):
                                    continue
                                if h == at:
                                    wait_apart(dve, s_x1, n + 1, s_wdve)
                                    nc.vector.bn_stats(st2[:], tile(X, n)).then_inc(s_st2, 1)
                                if h == at + 1:
                                    wait_apart(dve, s_st2, n + 1, s_wdve)
                                    nc.vector.bn_aggr(mvq[:], st2[:]).then_inc(s_mv2, 1)
                                if h == at + 2:
                                    dve.wait_ge(s_mv2, n + 1)
                                    nc.vector.tensor_scalar(tile(mv2, n), mvq[:], 1.0, None, ALU.mult)

                    for c in steps(body, dve.Fori):
                        if c == -1:
                            stats(EARLY, MIDDLE)
                        if c == 0:
                            dve.wait_ge(s_wt, 1)
                            nc.vector.tensor_copy(wpT[:], psum[:, 0, :].rearrange("p (a n) -> p a n", a=DT)).then_inc(s_wc, 1)
                            stats(MIDDLE, NT)
                            invert(EARLY, NT, 2)
                        if c == B:
                            for i in range(9):
                                dve.wait_ge(s_wt, i + 2)
                                src = psum[:, i % 2, :]
                                kind, j = divmod(i, 3)
                                if kind < 2:
                                    dst = (wgT, wuT)[kind][:, :, 2 * P * j:2 * P * (j + 1)]
                                    v = src.rearrange("p (a n) -> p a n", a=DT)
                                else:
                                    dst = wdT[:, 2 * j:2 * j + 2, :]
                                    v = src.rearrange("p (j n) -> p j n", j=2)
                                nc.vector.tensor_copy(dst, v).then_inc(s_wc, 1)

                @block.tensor
                def _(pe):
                    def body(c, par, fixed):
                        for h in range(HEADS):
                            g = h // GROUP
                            for t, at, b in ((0, 12, 2), (1, 4, 1)):
                                if h == at and live(fixed, -b):
                                    pe.wait_ge((s_norm, s_cn)[t], (QT, 1)[t] * (c + b + 1))
                                    if t == 1 or later(fixed, -b, 1):
                                        pe.wait_ge(s_r1, 2 * (c + b) + t)
                                    if t == 0 and later(fixed, 0, 0):
                                        pe.wait_ge(s_nr, c * NG + 2)
                                    if t == 1 and later(fixed, 0, 1):
                                        pe.wait_ge(s_nr, c * NG)
                                    for u in range(DT):
                                        for q in range(QT):
                                            last = nc.tensor.transpose(
                                                bank_in[:, (u * QT + q) * P:(u * QT + q + 1) * P],
                                                (xn, cn)[t][:, q, u * P:(u + 1) * P], ident[:])
                                    last.then_inc(s_inT, 1)
                            if live(fixed, 0):
                                if h % HALF == 0:
                                    pe.wait_ge(s_op[h // HALF], 16 * LOADS * (c + 1))
                                n = c * HEADS + h
                                if fixed != 0 or h >= NS:
                                    pe.wait_ge(s_max, n - NS + 1)
                                o = bank_s(h)
                                nc.tensor.matmul(o[:, 0:2 * BAND], identb[:], maskb[:], start=True, stop=False,
                                                 skip_group_check=True)
                                for q in range(QT):
                                    last = nc.tensor.matmul(
                                        o[:, q * BAND:(q + 1) * BAND], Q6[0:ROWS, par, h, q * P:(q + 1) * P],
                                        K6[0:ROWS, par, h, q * WINDOW:q * WINDOW + BAND],
                                        start=False, stop=q == QT - 1, skip_group_check=True)
                                last.then_inc(s_S, 1)
                            lag, hh = (1, h - ST_LAG + HEADS) if h < ST_LAG else (0, h - ST_LAG)
                            if live(fixed, lag):
                                p, n = (par + lag) % 2, (c - lag) * HEADS + hh
                                if hh % GROUP == 0:
                                    g1 = hh // GROUP
                                    pe.wait_ge(s_sh[g1 % 2], 16 * (2 * (c - lag) + g1 // 2 + 1))
                                if hh >= NST:
                                    pe.wait_ge(s_P, n - NST + 1)
                                elif later(fixed, lag, 1):
                                    back = next(i for i in range(HEADS) if (HEADS - 1 - i) % NST == hh)
                                    pe.wait_ge(s_P, n - hh - back)
                                o = bank_st(hh)
                                for q in range(QT):
                                    last = nc.tensor.matmul(
                                        o[:, q * BAND:(q + 1) * BAND], K6[0:ALLROWS, p, hh, q * P:(q + 1) * P],
                                        Q6[0:ALLROWS, p, hh, q * WINDOW:q * WINDOW + BAND],
                                        start=True, stop=True)
                                last.then_inc(s_ST, 1)
                            if h % GROUP == GROUP - 1 and live(fixed, 1):
                                p = 1 - par
                                pe.wait_ge(s_mk, GROUP * (NG * (c - 1) + g + 1))
                                if g > 0 or later(fixed, 1, 1):
                                    pe.wait_ge(s_ho, NG * (c - 1) + g)
                                if g == 0:
                                    pe.wait_ge(s_v, c)
                                for q in range(QT):
                                    for r in range(GROUP):
                                        hh = GROUP * g + r
                                        last = nc.tensor.matmul(
                                            bank_av[VW * r:VW * (r + 1), q * WINDOW:q * WINDOW + BAND],
                                            vals[:, p, q, hh, :], probs[:, hh, q * BAND:(q + 1) * BAND],
                                            start=q == 0, stop=q == QT - 1, skip_group_check=True)
                                last.then_inc(s_av, 1)
                            if h % GROUP == 2:
                                lag, g1 = (1, 3) if h == 2 else (0, g - 1)
                                if live(fixed, lag):
                                    pe.wait_ge(s_n2, (c - lag) * NG + g1 + 1)
                                    if g1 >= 1 or later(fixed, lag, 1):
                                        pe.wait_ge(s_nr, (c - lag) * NG + g1)
                                    if h == 2 and live(fixed, -1):
                                        pe.wait_ge(s_r1, 2 * (c + 1) + 1)
                                    if h == 6 and live(fixed, -1):
                                        pe.wait_ge(s_r1, 2 * (c + 1) + 2)
                                    if h == 14 and live(fixed, -2):
                                        pe.wait_ge(s_r1, 2 * (c + 2) + 1)
                                    for q in range(QT):
                                        last = nc.tensor.transpose(
                                            bank_neg[:, q * P:(q + 1) * P],
                                            neg[:, g1, q].rearrange("p s h -> p (s h)"), identb[:])
                                    last.then_inc(s_nT, 1)
                            for q, at in ((0, 1), (1, 9)):
                                n = (c - 2) * QT + q
                                if not live(fixed, 2):
                                    continue
                                if h == at:
                                    if q == 0:
                                        pe.wait_ge(s_ho, NG * (c - 1))
                                    if fixed != 2 or q > 0:
                                        pe.wait_ge(s_x1, n)
                                    for g1 in range(NG):
                                        last = nc.tensor.transpose(bank_y[:, g1 * P:(g1 + 1) * P],
                                                                   heads[:, par, g1, q * P:(q + 1) * P], ident[:])
                                    last.then_inc(s_hT, 1)
                                if h == at + 3:
                                    pe.wait_ge(s_y, n + 1)
                                    for u in range(DT):
                                        last = nc.tensor.transpose(
                                            bank_y[:, u * P:(u + 1) * P],
                                            y[:].rearrange("p h d -> p (h d)")[:, u * P:(u + 1) * P], ident[:])
                                    last.then_inc(s_yT, 1)
                                if h == at + 5:
                                    pe.wait_ge(s_yc, n + 1)
                                    for u in range(DT):
                                        last = nc.tensor.matmul(bank_y[:, 0:D], yT[:, u, :], wpT[:, u, :],
                                                                start=u == 0, stop=u == DT - 1)
                                    last.then_inc(s_pr, 1)

                    pe.wait_ge(s_const, 7)
                    for c in steps(body, pe.Fori):
                        if c == 0:
                            pe.wait_ge(s_w[2], 16)
                            for u in range(DT):
                                for v in range(DT):
                                    last = nc.tensor.transpose(psum[:, 0, (2 * u + v) * P:(2 * u + v + 1) * P],
                                                               wpraw[:, v, u * P:(u + 1) * P], ident[:])
                            last.then_inc(s_wt, 1)
                            pe.wait_ge(s_wc, 1)
                            pe.wait_ge(s_const, 11)
                            pe.wait_ge(s_ones, 1)
                        if c == B:
                            pe.wait_ge(s_wf, 3)
                            pe.wait_ge(s_max, B * HEADS)
                            for i in range(9):
                                if i >= 2:
                                    pe.wait_ge(s_wc, i)
                                o = psum[:, i % 2, :]
                                kind, j = divmod(i, 3)
                                for u in range(2):
                                    for v in range(2):
                                        if kind < 2:
                                            w = wraw[:, kind].bitcast(F32).rearrange("p (j d) -> p j d", d=D)
                                            src = w[:, 2 * j + v, u * P:(u + 1) * P]
                                        else:
                                            w = wraw[:, 2].bitcast(F32).rearrange("p (a d) -> p a d", d=HID)
                                            src = w[:, v, (2 * j + u) * P:(2 * j + u + 1) * P]
                                        last = nc.tensor.transpose(o[:, (2 * u + v) * P:(2 * u + v + 1) * P], src, ident[:])
                                last.then_inc(s_wt, 1)

        with ExitStack() as f:
            CH = 4
            TOK = CH * P
            NC = NT // CH
            ORDER = (0, 2, 1, 3)
            std2 = sb("std2", [P, NT], F32, f)
            xn2 = sb("xn2", [P, CH, D], F32, f)
            xh = sb("xh", [P, 2, DT, TOK], F16, f)
            xl = sb("xl", [P, 2, DT, TOK], F16, f)
            gs = sb("gs", [P, 2, TOK], F32, f)
            hf = sb("hf", [P, 2, TOK], F32, f)
            hh_ = sb("hh", [P, 2, HT, TOK], F32R, f)
            hl_ = sb("hl", [P, 2, HT, TOK], F32R, f)
            yo = sb("yo", [P, CH, D], F32, f)

            t_std = sem("std2_done", f)
            t_wsp = sem("waits2_of_sp", f)
            t_rs = sem("rstd2_done", f)
            t_n = sem("normed2", f)
            t_xT = sem("x2_transposed", f)
            t_xh = sem("x2_high_done", f)
            t_xl = sem("x2_low_done", f)
            t_g = sem("gate_ready", f)
            t_u = sem("up_ready", f)
            t_gs = sem("silu_done", f)
            t_h = sem("hidden_done", f)
            t_hh = sem("hidden_high_done", f)
            t_hl = sem("hidden_low_done", f)
            t_d = sem("down_ready", f)
            t_y = sem("y_done", f)
            t_o = [sem(f"y_stored{i}", f) for i in range(CH)]

            bx = psum[:, 0:2, :]

            def bg(j):
                return psum[:, 2 + j % 2, :]

            def bu(j):
                return psum[:, 4 + j % 2, :]

            def bd(t):
                return psum[:, 6 + t // 2, (t % 2) * D:(t % 2 + 1) * D]

            def chunks(body, fori):
                first, last = 2, 2 + 2 * ((NC - 1 - 2) // 2)
                for c in range(-1, first):
                    body(c, c % 2, c)
                with fori(first, last - 1, 2) as c:
                    body(c, 0, None)
                    body(c + 1, 1, None)
                for c in range(last, NC + 1):
                    body(c, c % 2, c)

            def on(fixed, lag):
                return fixed is None or 0 <= fixed - lag < NC

            with nc.Block() as block:

                @block.scalar
                def _(act):
                    nc.scalar.activation(std2[:], mv2[:, :, 1], ACT.Sqrt, bias=eps[:]).then_inc(t_std, 1)

                    def body(c, par, fixed):
                        for j in range(HT):
                            if on(fixed, 0):
                                n = c * HT + j
                                act.wait_ge(t_g, n + 1)
                                if fixed != 0 or j >= 2:
                                    act.wait_ge(t_h, n - 1)
                                nc.scalar.activation(gs[:, j % 2], bg(j), ACT.Silu, scale=WSCALE).then_inc(t_gs, 1)
                            lag, jj = (0, j - 1) if j else (1, HT - 1)
                            if on(fixed, lag):
                                act.wait_ge(t_h, (c - lag) * HT + jj + 1)
                                if jj == 0 and (fixed is None or fixed >= 2):
                                    act.wait_ge(t_d, CH * (c - 1))
                                nc.scalar.activation(hh_[:, (par + lag) % 2, jj], hf[:, jj % 2], ACT.Copy).then_inc(t_hh, 1)
                            if j == 3 and on(fixed, -1):
                                act.wait_ge(t_xT, c + 2)
                                if fixed is None or fixed >= 1:
                                    act.wait_ge(t_u, HT * c)
                                nc.scalar.activation(xh[:, 1 - par], bx, ACT.Copy).then_inc(t_xh, 1)

                    chunks(body, act.Fori)

                @block.gpsimd
                def _(pool):
                    def body(c, par, fixed):
                        for j in range(HT):
                            if on(fixed, 0):
                                pool.wait_ge(t_hh, c * HT + j + 1)
                                nc.gpsimd.tensor_tensor(hl_[:, par, j], hf[:, j % 2], hh_[:, par, j].bitcast(F32),
                                                        ALU.subtract).then_inc(t_hl, 1)

                    chunks(body, pool.Fori)

                @block.vector
                def _(dve):
                    dve.wait_ge(t_std, 1)
                    nc.vector.reciprocal(rstd2[:], std2[:]).then_inc(t_rs, 1)
                    dve.wait_ge(t_rs, 1)

                    def body(c, par, fixed):
                        for j in range(HT):
                            if j == 0 and on(fixed, -1):
                                if fixed is None or fixed >= 0:
                                    dve.wait_ge(t_xT, c + 1)
                                for t in range(CH):
                                    i = (c + 1) * CH + t
                                    nc.vector.tensor_scalar(xn2[:, t, :], tile(X, i), one(mv2, i, 0), col(rstd2, i),
                                                            ALU.subtract, ALU.mult).then_inc(t_n, 1)
                            if on(fixed, 0):
                                n = c * HT + j
                                dve.wait_ge(t_gs, n + 1)
                                dve.wait_ge(t_u, n + 1)
                                if fixed != 0 or j >= 2:
                                    dve.wait_ge(t_hl, n - 1)
                                nc.vector.tensor_tensor(hf[:, j % 2], gs[:, j % 2], bu(j), ALU.mult).then_inc(t_h, 1)
                            if j == 3 and on(fixed, -1):
                                dve.wait_ge(t_xh, c + 2)
                                nc.vector.tensor_tensor(xl[:, 1 - par], bx, xh[:, 1 - par], ALU.subtract).then_inc(t_xl, 1)
                            if 2 <= j <= CH + 1 and on(fixed, 1):
                                t = ORDER[j - 2]
                                dve.wait_ge(t_d, (c - 1) * CH + j - 1)
                                i = (c - 1) * CH + t
                                if fixed is None or fixed >= 2:
                                    dve.wait_ge(t_o[t], 16 * (c - 1))
                                nc.vector.scalar_tensor_tensor(
                                    out=yo[:, t, :], in0=bd(t), scalar=WSCALE * WSCALE, in1=tile(X, i),
                                    op0=ALU.mult, op1=ALU.add).then_inc(t_y, 1)

                    chunks(body, dve.Fori)

                @block.sync
                def _(sp):
                    flat = out.rearrange("b (q p) d -> (b q) p d", p=P)

                    def body(c, par, fixed):
                        if on(fixed, 1):
                            for k, t in enumerate(ORDER):
                                i = (c - 1) * CH + t
                                wait_apart(sp, t_y, (c - 1) * CH + k + 1, t_wsp)
                                dst = flat[i] if isinstance(i, int) else flat[bass.ds(i, 1)].rearrange("a p d -> (a p) d")
                                sp.dma_start(dst, yo[:, t, :]).then_inc(t_o[t], 16)

                    chunks(body, sp.Fori)
                    for t in range(CH):
                        sp.wait_ge(t_o[t], 16 * NC)

                @block.tensor
                def _(pe):
                    def body(c, par, fixed):
                        for j in range(HT):
                            if on(fixed, 0):
                                n = c * HT + j
                                if j == 0:
                                    pe.wait_ge(t_xl, c + 1)
                                for w, o, ready, free in ((wgT, bg(j), t_g, t_gs), (wuT, bu(j), t_u, t_h)):
                                    if fixed != 0 or j >= 2:
                                        pe.wait_ge(free, n - 1)
                                    for u in range(DT):
                                        for v, xx in enumerate((xh, xl)):
                                            last = nc.tensor.matmul(o, w[:, u, j * P:(j + 1) * P], xx[:, par, u, :],
                                                                    start=u == 0 and v == 0, stop=u == DT - 1 and v == 1)
                                    last.then_inc(ready, 1)
                            if j == 1 and on(fixed, -1):
                                pe.wait_ge(t_n, CH * (c + 2))
                                if fixed is None or fixed >= 0:
                                    pe.wait_ge(t_xl, c + 1)
                                for u in range(DT):
                                    for t in range(CH):
                                        last = nc.tensor.transpose(bx[:, u, t * P:(t + 1) * P],
                                                                   xn2[:, t, u * P:(u + 1) * P], ident[:])
                                last.then_inc(t_xT, 1)
                            if 1 <= j <= CH and on(fixed, 1):
                                k, t = j - 1, ORDER[j - 1]
                                if j == 1:
                                    pe.wait_ge(t_hl, HT * c)
                                if k >= 2 or fixed is None or fixed >= 2:
                                    pe.wait_ge(t_y, CH * (c - 1) + k - 1)
                                for k in range(HT):
                                    for v, m in enumerate((hh_, hl_)):
                                        last = nc.tensor.matmul(bd(t), m[:, 1 - par, k, t * P:(t + 1) * P], wdT[:, k, :],
                                                                start=k == 0 and v == 0, stop=k == HT - 1 and v == 1)
                                last.then_inc(t_d, 1)

                    chunks(body, pe.Fori)


_INS = ['x', 'ctx_1024', 'L0_xattn_W_proj', 'L0_xattn_b_proj', 'L0_ffn_w_gate', 'L0_ffn_w_up', 'L0_ffn_w_down']


def kernel(**inputs):
    import numpy as np
    import concourse.bacc as bacc
    from concourse.bass_utils import run_bass_kernel_spmd

    nc = bacc.Bacc("TRN2", target_bir_lowering=False, num_devices=1)
    arrays, args = {}, []
    for name in _INS:
        a = np.ascontiguousarray(inputs[name])
        arrays[f"in_{name}"] = a
        args.append(nc.dram_tensor(f"in_{name}", a.shape, mybir.dt.from_np(a.dtype), kind="ExternalInput").ap())
    args.append(nc.dram_tensor("out_0", inputs["x"].shape, F32, kind="ExternalOutput").ap())
    block_kernel(nc, *args)
    r = run_bass_kernel_spmd(nc, [arrays], core_ids=[0])
    return r.results[0]["out_0"]
```
